# Optimizing a Trainium2 kernel written in Bass

```python
import numpy as np
import jax
import jax.numpy as jnp

def _softmax(x, axis=-1):
    return jax.nn.softmax(x, axis=axis)

def _gelu(x):
    return jax.nn.gelu(x, approximate=True)

def _silu(x):
    return jax.nn.silu(x)

def _sigmoid(x):
    return jax.nn.sigmoid(x)

def _layernorm(x, axis=-1, eps=1e-05):
    m = jnp.mean(x, axis=axis, keepdims=True)
    v = jnp.var(x, axis=axis, keepdims=True)
    return (x - m) / jnp.sqrt(v + eps)

def _scatter_add(tgt, idx, src, axis=0):
    return tgt.at[idx].add(src)

def _segment_sum(src, seg, n):
    return jax.ops.segment_sum(src, seg, n)
kernel_name = 'mk_seq_postln_d1_jaxref_r4_934021'

def setup_inputs(seed: int=0):
    np.random.seed(seed)
    _w = jnp.asarray

    def _L0_attn_setup():
        import jax, jax.numpy as jnp
        import numpy as np
        B, T, D_MODEL = (2, 256, 256)
        H, DEPTH = (8, 5)
        DH = D_MODEL // H
        key = jax.random.key(seed)
        k_x, k_wp, k_bp, k_wv, k_wo = jax.random.split(key, 5)
        x = jax.random.normal(k_x, (B, T, D_MODEL), dtype=jnp.float32)
        Wp = jax.random.normal(k_wp, (D_MODEL, H * DEPTH), dtype=jnp.float32) * 0.02
        bp = jnp.zeros((H * DEPTH,), dtype=jnp.float32)
        Wv = jax.random.normal(k_wv, (D_MODEL, D_MODEL), dtype=jnp.float32) * 0.02
        Wo = jax.random.normal(k_wo, (D_MODEL, D_MODEL), dtype=jnp.float32) * 0.02
        return {'x': x, 'Wp': Wp, 'bp': bp, 'Wv': Wv, 'Wo': Wo}
    _L0_attn_in = _L0_attn_setup()

    def _L0_ffn_setup():
        import jax, jax.numpy as jnp
        import numpy as np
        DIM = 256
        HIDDEN = 768
        SCALE = 1.0 / 127.0

        def _dequant(w_int, dtype):
            return w_int.astype(dtype) * jnp.asarray(SCALE, dtype)
        key = jax.random.key(seed)
        k_x, k_g, k_u, k_d = jax.random.split(key, 4)
        x = jax.random.normal(k_x, (4, 512, DIM), dtype=jnp.float32)
        w_gate = jax.random.randint(k_g, (HIDDEN, DIM), -127, 128, dtype=jnp.int32)
        w_up = jax.random.randint(k_u, (HIDDEN, DIM), -127, 128, dtype=jnp.int32)
        w_down = jax.random.randint(k_d, (DIM, HIDDEN), -127, 128, dtype=jnp.int32)
        return {'x': x, 'w_gate': w_gate, 'w_up': w_up, 'w_down': w_down}
    _L0_ffn_in = _L0_ffn_setup()
    _d = {'L0_attn_x': _L0_attn_in['x'], 'L0_attn_Wp': _L0_attn_in['Wp'], 'L0_attn_bp': _L0_attn_in['bp'], 'L0_attn_Wv': _L0_attn_in['Wv'], 'L0_attn_Wo': _L0_attn_in['Wo'], 'L0_ffn_w_gate': _L0_ffn_in['w_gate'], 'L0_ffn_w_up': _L0_ffn_in['w_up'], 'L0_ffn_w_down': _L0_ffn_in['w_down']}
    _x0 = _d['L0_attn_x']
    _d['L0_attn_x'] = jax.random.normal(jax.random.fold_in(jax.random.key(seed), 1), (8, 1024, 256), dtype=_x0.dtype)
    del _x0
    return _d

def reference(L0_attn_x, L0_attn_Wp, L0_attn_bp, L0_attn_Wv, L0_attn_Wo, L0_ffn_w_gate, L0_ffn_w_up, L0_ffn_w_down):

    def _L0_attn_ref(x, Wp, bp, Wv, Wo):
        import jax, jax.numpy as jnp
        import numpy as np
        B, T, D_MODEL = (2, 256, 256)
        H, DEPTH = (8, 5)
        DH = D_MODEL // H
        Bx, Tx, d = x.shape
        paths = jax.nn.sigmoid(x @ Wp + bp)
        paths = paths.reshape(Bx, Tx, H, DEPTH).transpose(0, 2, 1, 3)
        pq = paths[:, :, :, None, :]
        pk = paths[:, :, None, :, :]
        agree = pq * pk + (1.0 - pq) * (1.0 - pk)
        sim = jnp.cumprod(agree, axis=-1).sum(axis=-1) / DEPTH
        mask = jnp.triu(jnp.ones((Tx, Tx), dtype=bool), k=1)
        sim = jnp.where(mask[None, None], -jnp.inf, sim)
        attn = jax.nn.softmax(sim, axis=-1)
        V = (x @ Wv).reshape(Bx, Tx, H, DH).transpose(0, 2, 1, 3)
        ctx = jnp.einsum('bhqk,bhkd->bhqd', attn, V)
        ctx = ctx.transpose(0, 2, 1, 3).reshape(Bx, Tx, d)
        return ctx @ Wo

    def _L0_ffn_ref(x, w_gate, w_up, w_down):
        import jax, jax.numpy as jnp
        import numpy as np
        DIM = 256
        HIDDEN = 768
        SCALE = 1.0 / 127.0

        def _dequant(w_int, dtype):
            return w_int.astype(dtype) * jnp.asarray(SCALE, dtype)
        wg = _dequant(w_gate, x.dtype)
        wu = _dequant(w_up, x.dtype)
        wd = _dequant(w_down, x.dtype)
        gate = jnp.einsum('bsd,hd->bsh', x, wg)
        up = jnp.einsum('bsd,hd->bsh', x, wu)
        h = jax.nn.silu(gate) * up
        return jnp.einsum('bsh,dh->bsd', h, wd)
    x = L0_attn_x
    x = _layernorm(x + _L0_attn_ref(x, L0_attn_Wp, L0_attn_bp, L0_attn_Wv, L0_attn_Wo), axis=-1)
    x = _layernorm(x + _L0_ffn_ref(x, L0_ffn_w_gate, L0_ffn_w_up, L0_ffn_w_down), axis=-1)
    return x

_drawn_inputs = setup_inputs


def setup_inputs(seed=0):
    import zlib

    import numpy as np

    out = dict(_drawn_inputs(seed))
    spreads = {'L0_attn_bp': (0.0, 0.8)}
    factors = {'L0_attn_Wp': 8.0, 'L0_attn_Wv': 4.439, 'L0_attn_Wo': 4.431}
    for name, (base, spread) in spreads.items():
        noise = np.random.default_rng([zlib.crc32(name.encode()), seed]).standard_normal(out[name].shape)
        drawn = base * np.exp(spread * noise) if base else spread * noise
        out[name] = jnp.asarray(drawn.astype(out[name].dtype))
    for name, factor in factors.items():
        out[name] = (out[name] * factor).astype(out[name].dtype)
    return out
```

```python
from contextlib import ExitStack

import concourse.bass as bass
from concourse import mybir

P = 128
ALU = mybir.AluOpType
ACT = mybir.ActivationFunctionType
AX = mybir.AxisListType
F32 = mybir.dt.float32
F16 = mybir.dt.float16
BF16 = mybir.dt.bfloat16
I32 = mybir.dt.int32
RMAX = bass.bass_isa.ReduceOp.max

DEPTH = 5
NF = 2 ** DEPTH
QUANT = 1.0 / 127.0
EPS = 1e-5
CH = 512
P_SLOTS = 3
LAG = 2


def bank_plan(names):
    plan, seen = {}, [0, 0]
    for n, name in enumerate(names):
        plan[name] = (n % 2, seen[n % 2])
        seen[n % 2] += 1
    return plan, seen


def seq_postln_kernel(nc, x, xT, Wp, bp, Wv, Wo, wgT, wuT, wdT, out):
    B, T, D = x.shape
    H = Wp.shape[1] // DEPTH
    DH = D // H
    F = wgT.shape[1]
    NT = T // P
    KD = D // P
    NG = H // 4
    NC = T // CH
    TC = CH // P
    M1 = F // P
    HD = H * DEPTH
    assert DH == 32 and NF == 32 and KD == 2 and NG == 2 and NC == 2

    CHUNKS = [(c, g) for c in range(NC) for g in range(NG)]
    STEPS = [(q, c, g, j) for q, (c, g) in enumerate(CHUNKS) for j in range(TC * (c + 1))]
    NS = len(STEPS)
    DIAG = [i for i, (q, c, g, j) in enumerate(STEPS) if j >= TC * c]
    LAST = {q: max(i for i, s in enumerate(STEPS) if s[0] == q) for q in range(len(CHUNKS))}
    NQ = len(CHUNKS)
    STACK_DMAS = 4 * 2
    PAIR_USES = NS + NC * M1 // 2

    PRE = ["z"] + [f"v{n}" for n in range(NT // 2)] + [f"f{g}{c}" for g in range(NG) for c in range(NC)]
    SETUP = ["scale"]
    FIRST = SETUP + PRE
    TAIL = [f"d{c}{n}" for c in range(NC) for n in range(TC // 2)]
    WITH_NEXT = (["z", "o00", "o01", "x00", "x01"] + [f"v{n}" for n in range(NT // 2)] + ["o10", "o11"]
                 + [f"f{g}{c}" for g in range(NG) for c in range(NC)] + ["x10", "x11"] + TAIL)
    WITHOUT = ["o00", "o01", "x00", "x01", "o10", "o11", "x10", "x11"] + TAIL
    plan_first, n_first = bank_plan(FIRST)
    plan_next, n_next = bank_plan(WITH_NEXT)
    plan_last, _ = bank_plan(WITHOUT)

    with ExitStack() as ctx:
        def sb(name, shape, dt):
            return ctx.enter_context(nc.sbuf_tensor(name, shape, dt))

        def sem(name):
            return ctx.enter_context(nc.semaphore(name))

        xT_sb = sb("xT_sb", [P, KD, T], F32)
        x_sb = sb("x_sb", [P, NT, D], F32)
        v_sb = sb("v_sb", [P, NT, D], F32)
        z_sb = sb("z_sb", [P, NT, HD], F32)
        u_sb = sb("u_sb", [P, NT * H, DEPTH], F32)
        feat = sb("feat", [P, NT * H, NF], F32)
        phi_hi = sb("phi_hi", [P, NG, T], F16)
        phi_lo = sb("phi_lo", [P, NG, T], F16)
        key_stack = sb("key_stack", [P, H, T], F16)
        query_stack = sb("query_stack", [P, H, T], F16)
        probs = sb("probs", [P, P_SLOTS, 4, CH], F32)
        ctxT = sb("ctxT", [P, NG, CH], F32)
        ctx_raw = sb("ctx_raw", [P, CH], F32)
        den_raw = sb("den_raw", [P, CH], F32)
        den_inv = sb("den_inv", [P, CH], F32)
        x1 = sb("x1", [P, NT, D], F32)
        x1T_hi = sb("x1T_hi", [P, KD, T], F16)
        x1T_lo = sb("x1T_lo", [P, KD, T], F16)
        tanh_g = sb("tanh_g", [P, 2, CH], F32)
        gated = sb("gated", [P, 2, CH], F32)
        hid = sb("hid", [P, 2, CH], F32)
        hbuf = sb("hbuf", [P, 2 * NC * M1 * CH // 2], F32)
        half = NC * M1 * CH // 2
        hid_hi = hbuf[:, 0:half].bitcast(F16).rearrange("p (c m n) -> p c m n", c=NC, m=M1)
        hid_lo = hbuf[:, half:2 * half].bitcast(F16).rearrange("p (c m n) -> p c m n", c=NC, m=M1)
        WN = KD * F
        w_int = [hbuf[:, n * WN:(n + 1) * WN].bitcast(I32) for n in range(3)]
        w_rest = hbuf[:, 3 * WN:4 * WN]
        wv_sb = sb("wv_sb", [P, KD, D], F32)
        wp_sb = sb("wp_sb", [P, KD, HD], F32)
        bp_sb = sb("bp_sb", [P, HD], F32)
        wo_sb = sb("wo_sb", [P, KD, D], F32)
        w_parts = sb("w_parts", [P, 3, 3, WN], BF16)
        ident = sb("ident", [P, P], F32)
        ones = sb("ones", [P, 32], F32)
        scale_row = sb("scale_row", [1, P], F32)
        feat_scale = sb("feat_scale", [P, 1], F32)
        neg_half = sb("neg_half", [P, TC], F32)
        bn = sb("bn", [P, TC, 6], F32)
        mv = sb("mv", [P, TC, 2], F32)
        var_eps = sb("var_eps", [P, TC], F32)
        rstd = sb("rstd", [P, TC], F32)
        w_max = sb("w_max", [P, 4], F32)
        w_gmax = sb("w_gmax", [P, 4], F32)
        rest_max = sb("rest_max", [P, 3], F32)
        w_one = sb("w_one", [P, 2], F32)
        w_prod = sb("w_prod", [P, 1], F32)
        w_inv = sb("w_inv", [P, 1], F32)
        hid_scale = sb("hid_scale", [P, 1], F32)
        out_scale = sb("out_scale", [P, 1], F32)
        wide = sb("wide", [1, 1], I32)

        pair = [ctx.enter_context(nc.psum_tensor(f"pair{n}", [P, 2, CH], F32)) for n in range(2)]
        ctx_ps = ctx.enter_context(nc.psum_tensor("ctx_ps", [P, CH], F32))
        den_ps = ctx.enter_context(nc.psum_tensor("den_ps", [P, CH], F32))
        misc = [ctx.enter_context(nc.psum_tensor(f"misc{n}", [P, CH], F32)) for n in range(2)]

        xT_in = sem("xT_in")
        x_in = sem("x_in")
        weights_in = sem("weights_in")
        ints_in = sem("ints_in")
        phi_stored = sem("phi_stored")
        stacks_in = sem("stacks_in")
        out_stored = sem("out_stored")
        ident_ready = sem("ident_ready")
        consts_ready = sem("consts_ready")
        scale_ready = sem("scale_ready")
        misc_filled = [sem(f"misc{n}_filled") for n in range(2)]
        misc_drained = [sem(f"misc{n}_drained") for n in range(2)]
        pair_filled = [sem(f"pair{n}_filled") for n in range(2)]
        pair_drained = [sem(f"pair{n}_drained") for n in range(2)]
        u_ready = sem("u_ready")
        feat_ready = sem("feat_ready")
        v_ready = sem("v_ready")
        phi_hi_ready = sem("phi_hi_ready")
        masked = sem("masked")
        pv_done = sem("pv_done")
        ctx_out = sem("ctx_out")
        den_out = sem("den_out")
        den_inv_ready = sem("den_inv_ready")
        ctxT_ready = sem("ctxT_ready")
        bn_ready = sem("bn_ready")
        mv_ready = sem("mv_ready")
        var_ready = sem("var_ready")
        rstd_ready = sem("rstd_ready")
        ln_done = sem("ln_done")
        x1T_hi_ready = sem("x1T_hi_ready")
        tanh_ready = sem("tanh_ready")
        gated_ready = sem("gated_ready")
        hid_hi_ready = sem("hid_hi_ready")
        hid_lo_ready = sem("hid_lo_ready")
        split_step = sem("split_step")
        w_max_ready = sem("w_max_ready")
        w_gmax_ready = sem("w_gmax_ready")
        ffn_scale_step = sem("ffn_scale_step")
        weights_split = sem("weights_split")

        def use(name, b, last=False):
            if b is None:
                return plan_first[name]
            k, n = (plan_last if last else plan_next)[name]
            return k, n_first[k] + b * n_next[k] + n

        phi_dram = nc.dram_tensor("phi_dram", (2, H * NF, T), F16, kind="Internal").ap()

        x_v = x.rearrange("b (t p) d -> b p t d", p=P)
        xT_v = xT.rearrange("b (k p) t -> b p k t", p=P)
        out_v = out.rearrange("b (t p) d -> b p t d", p=P)

        block = ctx.enter_context(nc.Block())

        @block.sync
        def _(sp):
            def load_xT(b):
                sp.dma_start(xT_sb[:, :, :], xT_v[b, :, :, :]).then_inc(xT_in, 16)

            def load_x(b):
                sp.dma_start(x_sb[:, :, :], x_v[b, :, :, :]).then_inc(x_in, 16)

            def stacks(b, it):
                for g in range(NG):
                    k, n = use(f"f{g}{NC - 1}", it)
                    sp.wait_ge(misc_drained[k], n + 1)
                    for r, part in enumerate((phi_hi, phi_lo)):
                        sp.dma_start(phi_dram[r, g * P:(g + 1) * P, :], part[:, g, :]).then_inc(phi_stored, 16)
                sp.wait_ge(phi_stored, 16 * 2 * NG * (b + 1))
                rows = [phi_dram[r, :, :].rearrange("(h p) n -> p h n", p=NF) for r in range(2)]
                for q in range(4):
                    for stack, r in ((key_stack, q // 2), (query_stack, q % 2)):
                        sp.dma_start(stack[32 * q:32 * q + 32, :, :], rows[r]).then_inc(stacks_in, 16)

            load_xT(0)
            sp.dma_start(wp_sb[:, :, :], Wp.rearrange("(k p) n -> p k n", p=P)).then_inc(weights_in, 16)
            sp.dma_start(bp_sb[:, :], bp.rearrange("(a n) -> a n", a=1).partition_broadcast(P)).then_inc(weights_in, 16)
            sp.dma_start(wv_sb[:, :, :], Wv.rearrange("(k p) n -> p k n", p=P)).then_inc(weights_in, 16)
            sp.dma_start(wo_sb[:, :, :], Wo.rearrange("(k p) n -> p k n", p=P)).then_inc(weights_in, 16)
            load_x(0)
            for n, w in enumerate((wgT, wuT)):
                sp.dma_start(w_int[n].rearrange("p (k n) -> p k n", k=KD),
                             w.rearrange("(k p) n -> p k n", p=P)).then_inc(ints_in, 16)
            sp.dma_start(w_int[2].rearrange("p (m n) -> p m n", m=M1),
                         wdT.rearrange("(m p) n -> p m n", p=P)).then_inc(ints_in, 16)
            stacks(0, None)

            def batch(b, last):
                if not last:
                    sp.wait_ge(v_ready, (NT // 2) * (b + 1))
                    load_xT(b + 1)
                    stacks(b + 1, b)
                for c in range(NC):
                    sp.wait_ge(ln_done, 4 * TC * b + 2 * TC + TC * (c + 1))
                    sp.dma_start(out_v[b, :, TC * c:TC * (c + 1), :],
                                 x1[:, TC * c:TC * (c + 1), :]).then_inc(out_stored, 16)
                if not last:
                    sp.wait_ge(out_stored, 16 * NC * (b + 1))
                    load_x(b + 1)

            with sp.Fori(0, B - 1) as b:
                batch(b, False)
            batch(B - 1, True)
            sp.wait_ge(out_stored, 16 * NC * B)

        @block.gpsimd
        def _(pool):
            pool.memset(ident[:, :], 0.0).then_inc(ident_ready, 1)
            pool.memset(neg_half[:, :], -0.5).then_inc(consts_ready, 1)
            pool.memset(ones[:, :], 1.0).then_inc(consts_ready, 1)
            pool.wait_ge(ident_ready, 1)
            pool.affine_select(out=ident[:, :], in_=ident[:, :], compare_op=ALU.not_equal, fill=1.0,
                               base=0, pattern=[[-1, P]], channel_multiplier=1).then_inc(ident_ready, 1)
            pool.wait_ge(w_max_ready, 4)
            pool.partition_all_reduce(w_gmax[:, :], w_max[:, :], P, RMAX).then_inc(w_gmax_ready, 1)

            def mask(i, b):
                q, c, g, j = STEPS[i]
                off = P * j - CH * c
                steps_done = pool.compute_val(PAIR_USES * b + i + 1)
                pool.wait_ge(ident_ready, 2)
                pool.wait_ge(pair_drained[0], steps_done)
                pool.wait_ge(pair_drained[1], steps_done)
                tile = probs[:, i % P_SLOTS, :, off:off + P]
                pool.affine_select(out=tile, in_=tile, compare_op=ALU.is_ge, fill=0.0, base=0,
                                   pattern=[[0, 4], [1, P]], channel_multiplier=-1).then_inc(masked, 1)

            def rsqrt(n, b):
                pool.wait_ge(var_ready, 4 * b + n + 1)
                pool.tensor_tensor(rstd[:, :], var_eps[:, :], neg_half[:, :], ALU.pow).then_inc(rstd_ready, 1)

            def hidden_lo(c, m, b):
                n = c * M1 + m
                pool.wait_ge(hid_hi_ready, NC * M1 * b + n + 1)
                pool.tensor_tensor(hid_lo[:, c, m, :], hid[:, n % 2, :], hid_hi[:, c, m, :],
                                   ALU.subtract).then_inc(hid_lo_ready, 1)

            def batch(b, last):
                for i in range(NS):
                    if i in DIAG:
                        mask(i, b)
                    if i == LN_A0:
                        rsqrt(0, b)
                rsqrt(1, b)
                for c in range(NC):
                    for m in range(M1):
                        hidden_lo(c, m, b)
                for c in range(NC):
                    rsqrt(2 + c, b)

            with pool.Fori(0, B - 1) as b:
                batch(b, False)
            batch(B - 1, True)

        @block.scalar
        def _(act):
            def squash(it, b):
                k, n = use("z", it)
                act.wait_ge(misc_drained[k], n + 1)
                act.activation(u_sb[:, :, :].rearrange("p a d -> p (a d)"),
                               z_sb[:, :, :].rearrange("p t n -> p (t n)"),
                               ACT.Tanh, scale=0.5).then_inc(u_ready, 1)

            def values(it, b):
                for s in range(NT // 2):
                    k, n = use(f"v{s}", it)
                    act.wait_ge(misc_filled[k], n + 1)
                    act.activation(v_sb[:, 2 * s:2 * s + 2, :].rearrange("p t n -> p (t n)"),
                                   misc[k][:, :], ACT.Copy).then_inc(misc_drained[k], 1)
                    act.wait_ge(misc_drained[k], n + 1)
                    act.sem_inc(v_ready, 1)

            def phi_high(it, b):
                for g in range(NG):
                    for c in range(NC):
                        k, n = use(f"f{g}{c}", it)
                        act.wait_ge(misc_filled[k], n + 1)
                        if g == 0 and c == 0:
                            act.wait_ge(scale_ready, 1)
                            if it is not None:
                                act.wait_ge(stacks_in, 16 * STACK_DMAS * b)
                        act.activation(phi_hi[:, g, CH * c:CH * (c + 1)], misc[k][:, :], ACT.Copy,
                                       scale=feat_scale[:, 0:1]).then_inc(phi_hi_ready, 1)

            def exps(i, b):
                q, c, g, j = STEPS[i]
                off = max(P * j - CH * c, 0)
                if i >= P_SLOTS:
                    act.wait_ge(pv_done, NS * b + i - P_SLOTS + 1)
                for p in range(2):
                    act.wait_ge(pair_filled[p], PAIR_USES * b + i + 1)
                    act.activation(probs[:, i % P_SLOTS, 2 * p:2 * p + 2, off:CH],
                                   pair[p][:, :, off:CH], ACT.Exp).then_inc(pair_drained[p], 1)

            def x1_high(c, b, last):
                for k2 in range(KD):
                    k, n = use(f"x{c}{k2}", b, last)
                    act.wait_ge(misc_filled[k], n + 1)
                    act.activation(x1T_hi[:, k2, CH * c:CH * (c + 1)], misc[k][:, :],
                                   ACT.Copy).then_inc(x1T_hi_ready, 1)

            def gate_tanh(c, m, b):
                n = c * M1 + m
                act.wait_ge(pair_filled[n % 2], PAIR_USES * b + NS + n // 2 + 1)
                act.activation(tanh_g[:, n % 2, :], pair[n % 2][:, 0, :], ACT.Tanh,
                               scale=0.5 * QUANT).then_inc(tanh_ready, 1)

            def hidden_hi(c, m, b):
                n = c * M1 + m
                act.wait_ge(pair_drained[n % 2], PAIR_USES * b + NS + n // 2 + 1)
                act.activation(hid_hi[:, c, m, :], hid[:, n % 2, :], ACT.Copy).then_inc(hid_hi_ready, 1)

            squash(None, 0)
            values(None, 0)
            phi_high(None, 0)

            def batch(b, last):
                for i in range(NS):
                    exps(i, b)
                    if i == Z_AT and not last:
                        squash(b, b + 1)
                    if i == XT0_AT:
                        x1_high(0, b, last)
                if not last:
                    values(b, b + 1)
                    phi_high(b, b + 1)
                for n in range(NC * M1 + 1):
                    if n < NC * M1:
                        gate_tanh(n // M1, n % M1, b)
                    if n >= 1:
                        hidden_hi((n - 1) // M1, (n - 1) % M1, b)
                    if n == M1 - 2:
                        x1_high(1, b, last)

            with act.Fori(0, B - 1) as b:
                batch(b, False)
            batch(B - 1, True)

        @block.vector
        def _(dve):
            def bias_add(it, b):
                k, n = use("z", it)
                dve.wait_ge(misc_filled[k], n + 1)
                dve.tensor_tensor(z_sb[:, :, :], misc[k][:, 0:NT * HD].rearrange("p (t n) -> p t n", t=NT),
                                  bp_sb[:, :].rearrange("p (a n) -> p a n", a=1).to_broadcast([P, NT, HD]),
                                  ALU.add).then_inc(misc_drained[k], 1)

            def features(b, levels):
                for m in levels:
                    w = 2 ** m
                    if m == 0:
                        dve.wait_ge(u_ready, b + 1)
                    dve.wait_ge(feat_ready, DEPTH * b + m)
                    dve.tensor_tensor(feat[:, :, w:2 * w], feat[:, :, 0:w],
                                      u_sb[:, :, m:m + 1].to_broadcast([P, NT * H, w]),
                                      ALU.mult).then_inc(feat_ready, 1)

            def phi_low(it, b):
                for s in range(NG * NC):
                    g, c = divmod(s, NC)
                    k, n = use(f"f{g}{c}", it)
                    cols = slice(CH * c, CH * (c + 1))
                    dve.wait_ge(phi_hi_ready, NG * NC * b + s + 1)
                    dve.scalar_tensor_tensor(out=phi_lo[:, g, cols], in0=misc[k][:, :],
                                             scalar=feat_scale[:, 0:1], in1=phi_hi[:, g, cols],
                                             op0=ALU.mult, op1=ALU.subtract).then_inc(misc_drained[k], 1)

            def normalise(q, b):
                c, g = CHUNKS[q]
                dve.wait_ge(pv_done, NS * b + LAST[q] + 1)
                if q >= 1:
                    dve.wait_ge(ctxT_ready, NQ * b + q)
                dve.tensor_copy(ctx_raw[:, :], ctx_ps[:, :]).then_inc(ctx_out, 1)
                dve.tensor_copy(den_raw[:, :], den_ps[:, :]).then_inc(den_out, 1)
                dve.wait_ge(den_out, NQ * b + q + 1)
                dve.reciprocal(den_inv[:, :], den_raw[:, :]).then_inc(den_inv_ready, 1)
                dve.wait_ge(den_inv_ready, NQ * b + q + 1)
                dve.wait_ge(ctx_out, NQ * b + q + 1)
                dve.tensor_tensor(ctxT[:, g, :], ctx_raw[:, :], den_inv[:, :], ALU.mult)\
                    .then_inc(ctxT_ready, 1)

            def residual(c, b, last):
                for s in range(TC // 2):
                    k, n = use(f"o{c}{s}", b, last)
                    t = TC * c + 2 * s
                    dve.wait_ge(misc_filled[k], n + 1)
                    if s == 0 and c == 0:
                        dve.wait_ge(x_in, 16 * (b + 1))
                    dve.tensor_tensor(x1[:, t:t + 2, :], misc[k][:, :].rearrange("p (t n) -> p t n", t=2),
                                      x_sb[:, t:t + 2, :], ALU.add).then_inc(misc_drained[k], 1)

            def ffn_residual(c, b, last):
                for s in range(TC // 2):
                    k, n = use(f"d{c}{s}", b, last)
                    t = TC * c + 2 * s
                    dve.wait_ge(misc_filled[k], n + 1)
                    dve.scalar_tensor_tensor(out=x1[:, t:t + 2, :].rearrange("p t n -> p (t n)"),
                                             in0=misc[k][:, :], scalar=out_scale[:, 0:1],
                                             in1=x1[:, t:t + 2, :].rearrange("p t n -> p (t n)"),
                                             op0=ALU.mult, op1=ALU.add).then_inc(misc_drained[k], 1)

            def ln_stats(kind, c, b, last):
                ln = NC * kind + c
                if ln >= 1:
                    dve.wait_ge(ln_done, 4 * TC * b + TC * ln)
                for s in range(TC // 2):
                    k, n = use(f"{'od'[kind]}{c}{s}", b, last)
                    dve.wait_ge(misc_drained[k], n + 1)
                    for t in (2 * s, 2 * s + 1):
                        dve.bn_stats(bn[:, t, :], x1[:, TC * c + t, :]).then_inc(bn_ready, 1)
                rows_done = dve.compute_val(4 * TC * b + TC * (ln + 1))
                dve.wait_ge(weights_in, 16 * 4)
                dve.wait_ge(bn_ready, rows_done)
                for t in range(TC):
                    dve.bn_aggr(mv[:, t, :], bn[:, t, :]).then_inc(mv_ready, 1)
                dve.wait_ge(mv_ready, 4 * TC * b + TC * ln + TC)
                dve.tensor_scalar(var_eps[:, :], mv[:, :, 1], EPS, None, ALU.add).then_inc(var_ready, 1)

            def ln_apply(kind, c, b):
                ln = NC * kind + c
                dve.wait_ge(rstd_ready, 4 * b + ln + 1)
                for t in range(TC):
                    row = x1[:, TC * c + t, :]
                    dve.tensor_scalar(row, row, mv[:, t, 0:1], rstd[:, t:t + 1],
                                      ALU.subtract, ALU.mult).then_inc(ln_done, 1)

            def x1_low(c, b, last):
                for k2 in range(KD):
                    k, n = use(f"x{c}{k2}", b, last)
                    cols = slice(CH * c, CH * (c + 1))
                    dve.wait_ge(x1T_hi_ready, NC * KD * b + KD * c + k2 + 1)
                    dve.tensor_tensor(x1T_lo[:, k2, cols], misc[k][:, :], x1T_hi[:, k2, cols],
                                      ALU.subtract).then_inc(misc_drained[k], 1)

            def hidden(c, m, b):
                n = c * M1 + m
                p, s = n % 2, n % 2
                dve.wait_ge(tanh_ready, NC * M1 * b + n + 1)
                dve.wait_ge(pair_drained[p], PAIR_USES * b + NS + n // 2)
                dve.scalar_tensor_tensor(out=gated[:, s, :], in0=tanh_g[:, s, :], scalar=1.0,
                                         in1=pair[p][:, 0, :], op0=ALU.add, op1=ALU.mult)\
                    .then_inc(gated_ready, 1)
                dve.wait_ge(gated_ready, NC * M1 * b + n + 1)
                if n >= 2:
                    dve.wait_ge(hid_lo_ready, NC * M1 * b + n - 1)
                dve.scalar_tensor_tensor(out=hid[:, s, :], in0=gated[:, s, :], scalar=hid_scale[:, 0:1],
                                         in1=pair[p][:, 1, :], op0=ALU.mult, op1=ALU.mult)\
                    .then_inc(pair_drained[p], 1)

            dve.memset(feat[:, :, 0:1], 1.0)
            row = scale_row[:, :].rearrange("a (h f) -> a h f", h=4)
            for m in range(DEPTH + 1):
                c_m = sum(2.0 ** -l for l in range(max(m, 1), DEPTH + 1)) / DEPTH
                lo, hi = (0, 1) if m == 0 else (2 ** (m - 1), 2 ** m)
                ins = dve.memset(row[:, :, lo:hi], c_m ** 0.5)
            ins.then_inc(consts_ready, 1)
            k, n = use("scale", None)
            dve.wait_ge(misc_filled[k], n + 1)
            dve.tensor_copy(feat_scale[:, :], misc[k][:, 0:1]).then_inc(misc_drained[k], 1)
            dve.wait_ge(misc_drained[k], n + 1)
            dve.sem_inc(scale_ready, 1)
            dve.wait_ge(weights_in, 16 * 4)
            bias_add(None, 0)
            features(0, range(DEPTH))
            phi_low(None, 0)

            dve.wait_ge(ints_in, 16 * 3)
            for n in range(3):
                dve.tensor_copy(w_parts[:, n, 0, :], w_int[n]).then_inc(split_step, 1)
                dve.tensor_reduce(w_max[:, n:n + 1], w_int[n], AX.X, ALU.max,
                                  apply_absolute_value=True).then_inc(w_max_ready, 1)
                dve.wait_ge(split_step, 3 * n + 1)
                dve.tensor_tensor(w_rest[:, :], w_int[n], w_parts[:, n, 0, :], ALU.subtract)\
                    .then_inc(split_step, 1)
                dve.wait_ge(split_step, 3 * n + 2)
                dve.tensor_reduce(rest_max[:, n:n + 1], w_rest[:, :], AX.X, ALU.max,
                                  apply_absolute_value=True).then_inc(split_step, 1)
                dve.wait_ge(split_step, 3 * n + 3)
            dve.tensor_reduce(w_max[:, 3:4], rest_max[:, :], AX.X, ALU.max).then_inc(w_max_ready, 1)

            dve.wait_ge(w_gmax_ready, 1)
            chain = 0

            def scaled(ins):
                nonlocal chain
                chain += 1
                ins.then_inc(ffn_scale_step, 1)
                dve.wait_ge(ffn_scale_step, chain)

            scaled(dve.tensor_scalar(w_one[:, :], w_gmax[:, 0:2], 1.0, None, ALU.max))
            scaled(dve.tensor_tensor(w_prod[:, :], w_one[:, 0:1], w_one[:, 1:2], ALU.mult))
            scaled(dve.reciprocal(w_inv[:, :], w_prod[:, :]))
            scaled(dve.tensor_scalar(hid_scale[:, :], w_inv[:, :], 0.25, None, ALU.mult))
            scaled(dve.tensor_scalar(out_scale[:, :], w_prod[:, :], 2.0 * QUANT ** 3, None, ALU.mult))
            scaled(dve.tensor_scalar(wide[:, :], w_gmax[0:1, 3:4], 0.0, None, ALU.is_gt))
            rest_left = dve.value_load(wide[0:1, 0:1], min_val=0, max_val=1)
            with dve.If(rest_left == 1):
                steps = 9
                for n in range(3):
                    dve.tensor_tensor(w_rest[:, :], w_int[n], w_parts[:, n, 0, :], ALU.subtract)\
                        .then_inc(split_step, 1)
                    dve.wait_ge(split_step, steps + 4 * n + 1)
                    dve.tensor_copy(w_parts[:, n, 1, :], w_rest[:, :]).then_inc(split_step, 1)
                    dve.wait_ge(split_step, steps + 4 * n + 2)
                    dve.tensor_tensor(w_rest[:, :], w_rest[:, :], w_parts[:, n, 1, :], ALU.subtract)\
                        .then_inc(split_step, 1)
                    dve.wait_ge(split_step, steps + 4 * n + 3)
                    dve.tensor_copy(w_parts[:, n, 2, :], w_rest[:, :]).then_inc(split_step, 1)
                    dve.wait_ge(split_step, steps + 4 * n + 4)
            dve.end_ifs()
            dve.tensor_copy(w_one[:, :], w_gmax[:, 0:2]).then_inc(weights_split, 1)

            def batch(b, last):
                for i in range(NS + LAG):
                    if i == Z_AT and not last:
                        bias_add(b, b + 1)
                    if not last and Z_AT < i <= Z_AT + DEPTH:
                        features(b + 1, [i - Z_AT - 1])
                    for q in range(NQ):
                        if i == LAST[q] + LAG:
                            normalise(q, b)
                    if i == LN_A0:
                        residual(0, b, last)
                        ln_stats(0, 0, b, last)
                    if i == LN_A0 + 1:
                        ln_apply(0, 0, b)
                    if i == XT0_AT:
                        x1_low(0, b, last)
                residual(1, b, last)
                ln_stats(0, 1, b, last)
                if not last:
                    phi_low(b, b + 1)
                ln_apply(0, 1, b)
                for n in range(NC * M1):
                    if n == M1 - 1:
                        x1_low(1, b, last)
                    hidden(n // M1, n % M1, b)
                for c in range(NC):
                    ffn_residual(c, b, last)
                    ln_stats(1, c, b, last)
                    ln_apply(1, c, b)

            with dve.Fori(0, B - 1) as b:
                batch(b, False)
            batch(B - 1, True)

        @block.tensor
        def _(pe):
            def claim(name, it, last=False):
                k, n = use(name, it, last)
                if it is not None or n > 0:
                    pe.wait_ge(misc_drained[k], n)
                return k

            def paths(it, b):
                k = claim("z", it)
                pe.wait_ge(xT_in, 16 * (b + 1))
                for t in range(NT):
                    for d in range(KD):
                        mm = pe.matmul(misc[k][:, t * HD:(t + 1) * HD], xT_sb[:, d, t * P:(t + 1) * P],
                                       wp_sb[:, d, :], start=(d == 0), stop=(d == KD - 1))
                mm.then_inc(misc_filled[k], 1)

            def values(it, b):
                for s in range(NT // 2):
                    k = claim(f"v{s}", it)
                    for t in (2 * s, 2 * s + 1):
                        for d in range(KD):
                            mm = pe.matmul(misc[k][:, (t % 2) * D:(t % 2 + 1) * D],
                                           xT_sb[:, d, t * P:(t + 1) * P], wv_sb[:, d, :],
                                           start=(d == 0), stop=(d == KD - 1))
                    mm.then_inc(misc_filled[k], 1)

            def turn_features(it, b):
                pe.wait_ge(feat_ready, DEPTH * (b + 1))
                tiles = feat[:, :, :].rearrange("p (t h) f -> p t (h f)", h=H)
                for g in range(NG):
                    for c in range(NC):
                        k = claim(f"f{g}{c}", it)
                        for t in range(TC):
                            mm = pe.transpose(misc[k][:, t * P:(t + 1) * P],
                                              tiles[:, TC * c + t, g * P:(g + 1) * P], ident[:, :])
                        mm.then_inc(misc_filled[k], 1)

            def scores(i, b):
                q, c, g, j = STEPS[i]
                off = max(P * j - CH * c, 0)
                if i == 0:
                    pe.wait_ge(stacks_in, 16 * STACK_DMAS * (b + 1))
                for p in range(2):
                    if i >= 1:
                        pe.wait_ge(pair_drained[p], PAIR_USES * b + i)
                    for s in range(2):
                        h = 4 * g + 2 * p + s
                        mm = pe.matmul(pair[p][:, s, off:CH], key_stack[:, h, P * j:P * (j + 1)],
                                       query_stack[:, h, CH * c + off:CH * (c + 1)], start=True, stop=True)
                    mm.then_inc(pair_filled[p], 1)

            def weigh(i, b):
                q, c, g, j = STEPS[i]
                off = max(P * j - CH * c, 0)
                first, final = j == 0, j == TC * (c + 1) - 1
                if i == 0:
                    pe.wait_ge(v_ready, (NT // 2) * (b + 1))
                for p in range(2):
                    pe.wait_ge(pair_drained[p], PAIR_USES * b + i + 1)
                if i in DIAG:
                    pe.wait_ge(masked, len(DIAG) * b + DIAG.index(i) + 1)
                for bank, taken in ((ctx_ps, ctx_out), (den_ps, den_out)):
                    if first and q >= 1:
                        pe.wait_ge(taken, NQ * b + q)
                    for s in range(4):
                        h = 4 * g + s
                        w = v_sb[:, j, 32 * h:32 * h + 32] if bank is ctx_ps else ones[:, :]
                        mm = pe.matmul(bank[32 * s:32 * s + 32, off:CH], w,
                                       probs[:, i % P_SLOTS, s, off:CH], start=first, stop=final)
                mm.then_inc(pv_done, 1)

            def project(c, b, last):
                pe.wait_ge(ctxT_ready, NQ * b + NG * (c + 1))
                for s in range(TC // 2):
                    k = claim(f"o{c}{s}", b, last)
                    for t in (2 * s, 2 * s + 1):
                        for g in range(NG):
                            mm = pe.matmul(misc[k][:, (t % 2) * D:(t % 2 + 1) * D],
                                           ctxT[:, g, t * P:(t + 1) * P], wo_sb[:, g, :],
                                           start=(g == 0), stop=(g == NG - 1))
                    mm.then_inc(misc_filled[k], 1)

            def turn_x1(c, b, last):
                pe.wait_ge(ln_done, 4 * TC * b + TC * (c + 1))
                for k2 in range(KD):
                    k = claim(f"x{c}{k2}", b, last)
                    for t in range(TC):
                        mm = pe.transpose(misc[k][:, t * P:(t + 1) * P],
                                          x1[:, TC * c + t, k2 * P:(k2 + 1) * P], ident[:, :])
                    mm.then_inc(misc_filled[k], 1)

            def gate_up(c, m, b, parts):
                n = c * M1 + m
                p = n % 2
                pe.wait_ge(pair_drained[p], PAIR_USES * b + NS + n // 2)
                for w in range(2):
                    terms = [(a, k, d) for k in range(parts) for d in range(KD) for a in (x1T_hi, x1T_lo)]
                    for s, (a, k, d) in enumerate(terms):
                        mm = pe.matmul(pair[p][:, w, :], w_parts[:, w, k, d * F + m * P:d * F + (m + 1) * P],
                                       a[:, d, CH * c:CH * (c + 1)], start=(s == 0), stop=(s == len(terms) - 1))
                mm.then_inc(pair_filled[p], 1)

            def down(c, b, last, parts):
                pe.wait_ge(hid_lo_ready, NC * M1 * b + M1 * (c + 1))
                for s in range(TC // 2):
                    k = claim(f"d{c}{s}", b, last)
                    for t in (2 * s, 2 * s + 1):
                        terms = [(a, w, m) for w in range(parts) for m in range(M1) for a in (hid_hi, hid_lo)]
                        for e, (a, w, m) in enumerate(terms):
                            mm = pe.matmul(misc[k][:, (t % 2) * D:(t % 2 + 1) * D],
                                           a[:, c, m, t * P:(t + 1) * P],
                                           w_parts[:, 2, w, m * D:(m + 1) * D],
                                           start=(e == 0), stop=(e == len(terms) - 1))
                    mm.then_inc(misc_filled[k], 1)

            def feed_forward(b, last, parts):
                for c in range(NC):
                    k, n = use(f"x{c}{KD - 1}", b, last)
                    if c == 1:
                        turn_x1(1, b, last)
                    pe.wait_ge(misc_drained[k], n + 1)
                    for m in range(M1):
                        gate_up(c, m, b, parts)
                for c in range(NC):
                    down(c, b, last, parts)

            pe.wait_ge(consts_ready, 3)
            pe.wait_ge(ident_ready, 2)
            k, n = use("scale", None)
            pe.matmul(misc[k][:, 0:1], scale_row[:, :], ones[0:1, 0:1], start=True, stop=True)\
                .then_inc(misc_filled[k], 1)
            pe.wait_ge(weights_in, 16 * 4)
            paths(None, 0)
            values(None, 0)
            turn_features(None, 0)

            def batch(b, last):
                for i in range(NS + LAG):
                    if i < NS:
                        scores(i, b)
                    if i >= LAG:
                        weigh(i - LAG, b)
                    if i == Z_AT and not last:
                        paths(b, b + 1)
                    if i == LN_A0 - 1:
                        project(0, b, last)
                    if i == XT0_AT:
                        turn_x1(0, b, last)
                if not last:
                    values(b, b + 1)
                project(1, b, last)
                if not last:
                    turn_features(b, b + 1)
                pe.wait_ge(weights_split, 1)
                rest_left = pe.value_load(wide[0:1, 0:1], min_val=0, max_val=1)
                with pe.If(rest_left == 0):
                    feed_forward(b, last, 1)
                with pe.Else():
                    feed_forward(b, last, 3)

            with pe.Fori(0, B - 1) as b:
                batch(b, False)
            batch(B - 1, True)


Z_AT = 5
LN_A0 = 13
XT0_AT = 18

_OUTS = [((8, 1024, 256), 'float32')]


def kernel(L0_attn_x, L0_attn_Wp, L0_attn_bp, L0_attn_Wv, L0_attn_Wo, L0_ffn_w_gate, L0_ffn_w_up, L0_ffn_w_down):
    import numpy as _np
    import concourse.bacc as _bacc
    from concourse import mybir as _mybir
    from concourse.bass_utils import run_bass_kernel_spmd as _run

    lay = {
        "x": L0_attn_x,
        "xT": _np.asarray(L0_attn_x).transpose(0, 2, 1),
        "Wp": L0_attn_Wp, "bp": L0_attn_bp, "Wv": L0_attn_Wv, "Wo": L0_attn_Wo,
        "wgT": _np.asarray(L0_ffn_w_gate).T, "wuT": _np.asarray(L0_ffn_w_up).T,
        "wdT": _np.asarray(L0_ffn_w_down).T,
    }
    nc = _bacc.Bacc("TRN2", target_bir_lowering=False, num_devices=1)
    arrays, args = {}, []
    for name, a in lay.items():
        a = _np.ascontiguousarray(a)
        arrays[f"in_{name}_dram"] = a
        args.append(nc.dram_tensor(f"in_{name}_dram", a.shape, _mybir.dt.from_np(a.dtype), kind="ExternalInput").ap())
    for i, (shape, dtype) in enumerate(_OUTS):
        dt = _mybir.dt.from_np(_np.dtype(dtype))
        args.append(nc.dram_tensor(f"out_{i}_dram", shape, dt, kind="ExternalOutput").ap())
    seq_postln_kernel(nc, *args)
    r = _run(nc, [arrays], core_ids=[0])
    return r.results[0]["out_0_dram"]
```

```python
from contextlib import ExitStack

import concourse.bass as bass
from concourse import mybir

P = 128
ALU = mybir.AluOpType
ACT = mybir.ActivationFunctionType
AX = mybir.AxisListType
F32 = mybir.dt.float32
F16 = mybir.dt.float16
BF16 = mybir.dt.bfloat16
I32 = mybir.dt.int32
RMAX = bass.bass_isa.ReduceOp.max

DEPTH = 5
NF = 2 ** DEPTH
QUANT = 1.0 / 127.0
EPS = 1e-5
CH = 512
P_SLOTS = 3
HSLOTS = 3
LAG = 2


def bank_plan(names):
    plan, seen = {}, [0, 0]
    for n, name in enumerate(names):
        plan[name] = (n % 2, seen[n % 2])
        seen[n % 2] += 1
    return plan, seen


def seq_postln_kernel(nc, x, xT, Wp, bp, Wv, Wo, wgT, wuT, wdT, out):
    B, T, D = x.shape
    H = Wp.shape[1] // DEPTH
    DH = D // H
    F = wgT.shape[1]
    NT = T // P
    KD = D // P
    NG = H // 4
    NC = T // CH
    TC = CH // P
    M1 = F // P
    HD = H * DEPTH
    assert DH == 32 and NF == 32 and KD == 2 and NG == 2 and NC == 2

    CHUNKS = [(c, g) for c in range(NC) for g in range(NG)]
    STEPS = [(q, c, g, j) for q, (c, g) in enumerate(CHUNKS) for j in range(TC * (c + 1))]
    NS = len(STEPS)
    DIAG = [i for i, (q, c, g, j) in enumerate(STEPS) if j >= TC * c]
    LAST = {q: max(i for i, s in enumerate(STEPS) if s[0] == q) for q in range(len(CHUNKS))}
    NQ = len(CHUNKS)
    STACK_DMAS = 4 * 2
    SLOTS = 3
    GATES = NC * M1
    SLOT_USES = [NS + GATES // SLOTS, NS + GATES // SLOTS, GATES // SLOTS]
    VZ = D + HD
    HT = NT // 2

    def after_attention(batch_follows):
        plan = []
        if batch_follows:
            for t in range(NT):
                plan += [("vz", t), ("vz_out", t)]
                if t % HT == HT - 1:
                    plan += [("bias", t // HT), ("squash", t // HT), ("features", t // HT)]
        plan += [("project", 1), ("residual", 1), ("stats", 1), ("rsqrt", 1)]
        turn_at = {1: (0, 0), 2: (0, 1), 3: (1, 0), 4: (1, 1)} if batch_follows else {}
        for n in range(GATES):
            if n == X1_TURN_AT:
                plan += [("turn_x1", 1), ("x1_high", 1), ("x1_low", 1)]
            plan += [("gate_up", n), ("tanh", n)]
            if n >= 1:
                plan += [("hidden_hi", n - 1), ("hidden_lo", n - 1)]
            plan += [("hidden", n)]
            if n in turn_at:
                g, c = turn_at[n]
                plan += [("turn_features", g, c), ("phi_high", g, c), ("phi_low", g, c)]
                if c == NC - 1:
                    plan += [("stack", g)]
            if n == 0:
                plan += [("apply", 1)]
            if n == DOWN0_AT:
                plan += [("down", 0)]
        plan += [("ffn_residual", 0)]
        if batch_follows:
            plan += [("load_xT",), ("scores", 0), ("exps", 0)]
        plan += [("hidden_hi", GATES - 1), ("hidden_lo", GATES - 1)]
        if batch_follows:
            plan += [("scores", 1), ("exps", 1), ("mask", 0), ("mask", 1)]
        plan += [("stats", 2), ("rsqrt", 2), ("down", 1), ("apply", 2), ("store", 0)]
        if not batch_follows:
            plan += last_norm()
        return plan

    def last_norm():
        return [("ffn_residual", 1), ("stats", 3), ("rsqrt", 3), ("apply", 3), ("store", 1), ("load_x",)]

    def attention(first_batch):
        plan = []
        for i in range(LAG, NS + LAG):
            if i < NS:
                plan += [("scores", i), ("exps", i)]
                if i in DIAG:
                    plan += [("mask", i)]
            plan += [("weigh", i - LAG)]
            for q in range(NQ):
                if i == LAST[q] + LAG:
                    plan += [("normalise", q)]
            if i == LAST_NORM_AT and not first_batch:
                plan += last_norm()
            if i == PROJECT_AT:
                plan += [("project", 0), ("residual", 0), ("stats", 0), ("rsqrt", 0)]
            if i == PROJECT_AT + 1:
                plan += [("apply", 0)]
            if i == X1_AT:
                plan += [("turn_x1", 0), ("x1_high", 0), ("x1_low", 0)]
        return plan

    def first_projections():
        plan = [("scale",)]
        for t in range(NT):
            plan += [("vz", t), ("vz_out", t)]
            if t % HT == HT - 1:
                plan += [("bias", t // HT), ("squash", t // HT), ("features", t // HT)]
        for g in range(NG):
            for c in range(NC):
                plan += [("turn_features", g, c), ("phi_high", g, c), ("phi_low", g, c)]
            plan += [("stack", g)]
        plan += [("load_xT",), ("weights",)]
        for i in range(LAG):
            plan += [("scores", i), ("exps", i), ("mask", i)]
        return plan

    def misc_uses(plan):
        uses = []
        for what, *n in plan:
            if what == "scale":
                uses += ["scale"]
            elif what == "vz":
                uses += [f"vz{n[0]}"]
            elif what == "project":
                uses += [f"o{n[0]}{s}" for s in range(TC // 2)]
            elif what == "turn_x1":
                uses += [f"x{n[0]}{k}" for k in range(KD)]
            elif what == "turn_features":
                uses += [f"f{n[0]}{n[1]}"]
            elif what == "down":
                uses += [f"d{n[0]}{s}" for s in range(TC // 2)]
        return uses

    START = first_projections() + attention(True)
    BODY = after_attention(True) + attention(False)
    END = after_attention(False)
    plan_start, n_start = bank_plan(misc_uses(START))
    plan_body, n_body = bank_plan(misc_uses(BODY))
    plan_end, _ = bank_plan(misc_uses(END))

    def start_bank(name):
        return plan_start[name]

    def body_bank(b):
        def bank(name):
            k, n = plan_body[name]
            return k, n_start[k] + b * n_body[k] + n
        return bank

    def end_bank(name):
        k, n = plan_end[name]
        return k, n_start[k] + (B - 1) * n_body[k] + n

    def gate_slot(n, b):
        s = n % SLOTS
        return s, SLOT_USES[s] * b + (NS if s < 2 else 0) + n // SLOTS

    with ExitStack() as ctx:
        def sb(name, shape, dt):
            return ctx.enter_context(nc.sbuf_tensor(name, shape, dt))

        def sem(name):
            return ctx.enter_context(nc.semaphore(name))

        xT_sb = sb("xT_sb", [P, KD, T], F32)
        x_sb = sb("x_sb", [P, NT, D], F32)
        vz_sb = sb("vz_sb", [P, NT, VZ], F32)
        z_sb = sb("z_sb", [P, NT, HD], F32)
        u_sb = sb("u_sb", [P, NT * H, DEPTH], F32)
        feat = sb("feat", [P, NT * H, NF], F32)
        phi_hi = sb("phi_hi", [P, NG, T], F16)
        phi_lo = sb("phi_lo", [P, NG, T], F16)
        key_stack = sb("key_stack", [P, H, T], F16)
        query_stack = sb("query_stack", [P, H, T], F16)
        probs = sb("probs", [P, P_SLOTS, 4, CH], F32)
        ctxT = sb("ctxT", [P, NG, CH], F32)
        ctx_raw = sb("ctx_raw", [P, CH], F32)
        den_turned = sb("den_turned", [P, CH // 32, 32], F32)
        den_recip = sb("den_recip", [P, CH // 32, 1], F32)
        den_inv = sb("den_inv", [P, CH], F32)
        x1 = sb("x1", [P, NT, D], F32)
        x1T_hi = sb("x1T_hi", [P, KD, T], F16)
        x1T_lo = sb("x1T_lo", [P, KD, T], F16)
        tanh_g = sb("tanh_g", [P, 2, CH], F32)
        gated = sb("gated", [P, 2, CH], F32)
        hid = sb("hid", [P, HSLOTS, CH], F32)
        hbuf = sb("hbuf", [P, 2 * NC * M1 * CH // 2], F32)
        half = NC * M1 * CH // 2
        hid_hi = hbuf[:, 0:half].bitcast(F16).rearrange("p (c m n) -> p c m n", c=NC, m=M1)
        hid_lo = hbuf[:, half:2 * half].bitcast(F16).rearrange("p (c m n) -> p c m n", c=NC, m=M1)
        WN = KD * F
        w_int = [hbuf[:, n * WN:(n + 1) * WN].bitcast(I32) for n in range(3)]
        w_rest = hbuf[:, 3 * WN:4 * WN]
        wvp_sb = sb("wvp_sb", [P, KD, VZ], F32)
        bp_sb = sb("bp_sb", [P, HD], F32)
        wo_sb = sb("wo_sb", [P, KD, D], F32)
        w_parts = sb("w_parts", [P, 3, 3, WN], BF16)
        ident = sb("ident", [P, P], F32)
        ones = sb("ones", [P, 32], F32)
        scale_row = sb("scale_row", [1, P], F32)
        feat_scale = sb("feat_scale", [P, 1], F32)
        neg_half = sb("neg_half", [P, TC], F32)
        bn = sb("bn", [P, TC, 6], F32)
        mv = sb("mv", [P, TC, 2], F32)
        var_eps = sb("var_eps", [P, TC], F32)
        rstd = sb("rstd", [P, TC], F32)
        w_max = sb("w_max", [P, 4], F32)
        w_gmax = sb("w_gmax", [P, 4], F32)
        rest_max = sb("rest_max", [P, 3], F32)
        w_one = sb("w_one", [P, 2], F32)
        w_prod = sb("w_prod", [P, 1], F32)
        w_inv = sb("w_inv", [P, 1], F32)
        hid_scale = sb("hid_scale", [P, 1], F32)
        out_scale = sb("out_scale", [P, 1], F32)
        wide = sb("wide", [1, 1], I32)

        slot = [ctx.enter_context(nc.psum_tensor(f"slot{n}", [P, 2, CH], F32)) for n in range(SLOTS)]
        ctx_ps, den_ps = slot[2][:, 0, :], slot[2][:, 1, :]
        misc = [ctx.enter_context(nc.psum_tensor(f"misc{n}", [P, CH], F32)) for n in range(2)]

        xT_in = sem("xT_in")
        x_in = sem("x_in")
        weights_in = sem("weights_in")
        ints_in = sem("ints_in")
        wo_in = sem("wo_in")
        phi_stored = sem("phi_stored")
        stacks_in = [sem(f"stacks{g}_in") for g in range(NG)]
        out_stored = sem("out_stored")
        ident_ready = sem("ident_ready")
        consts_ready = sem("consts_ready")
        scale_ready = sem("scale_ready")
        misc_filled = [sem(f"misc{n}_filled") for n in range(2)]
        misc_drained = [sem(f"misc{n}_drained") for n in range(2)]
        slot_filled = [sem(f"slot{n}_filled") for n in range(SLOTS)]
        slot_drained = [sem(f"slot{n}_drained") for n in range(SLOTS)]
        z_ready = sem("z_ready")
        u_ready = sem("u_ready")
        feat_ready = sem("feat_ready")
        phi_hi_ready = sem("phi_hi_ready")
        masked = sem("masked")
        pv_done = sem("pv_done")
        ctx_out = sem("ctx_out")
        den_out = sem("den_out")
        den_recip_ready = sem("den_recip_ready")
        den_inv_ready = sem("den_inv_ready")
        ctxT_ready = sem("ctxT_ready")
        bn_ready = sem("bn_ready")
        mv_ready = sem("mv_ready")
        var_ready = sem("var_ready")
        rstd_ready = sem("rstd_ready")
        ln_done = sem("ln_done")
        x1T_hi_ready = sem("x1T_hi_ready")
        tanh_ready = sem("tanh_ready")
        gated_ready = sem("gated_ready")
        hid_hi_ready = sem("hid_hi_ready")
        hid_lo_ready = sem("hid_lo_ready")
        split_step = sem("split_step")
        w_max_ready = sem("w_max_ready")
        w_gmax_ready = sem("w_gmax_ready")
        ffn_scale_step = sem("ffn_scale_step")
        weights_split = sem("weights_split")

        phi_dram = nc.dram_tensor("phi_dram", (2, H * NF, T), F16, kind="Internal").ap()

        x_v = x.rearrange("b (t p) d -> b p t d", p=P)
        xT_v = xT.rearrange("b (k p) t -> b p k t", p=P)
        out_v = out.rearrange("b (t p) d -> b p t d", p=P)

        block = ctx.enter_context(nc.Block())

        @block.sync
        def _(sp):
            def load_xT(b):
                sp.wait_ge(u_ready, 2 * b)
                sp.dma_start(xT_sb[:, :, :], xT_v[b, :, :, :]).then_inc(xT_in, 16)

            def load_x(b):
                sp.wait_ge(out_stored, 16 * NC * b)
                sp.dma_start(x_sb[:, :, :], x_v[b, :, :, :]).then_inc(x_in, 16)

            def stack(g, b, bank):
                k, n = bank(f"f{g}{NC - 1}")
                sp.wait_ge(misc_drained[k], n + 1)
                for r, part in enumerate((phi_hi, phi_lo)):
                    sp.dma_start(phi_dram[r, g * P:(g + 1) * P, :], part[:, g, :]).then_inc(phi_stored, 16)
                sp.wait_ge(phi_stored, 16 * 2 * (NG * b + g + 1))
                for q in range(4):
                    for dest, r in ((key_stack, q // 2), (query_stack, q % 2)):
                        sp.dma_start(dest[32 * q:32 * q + 32, 4 * g:4 * g + 4, :],
                                     phi_dram[r, g * P:(g + 1) * P, :].rearrange("(h p) n -> p h n", p=NF))\
                            .then_inc(stacks_in[g], 16)

            def store(c, b):
                sp.wait_ge(ln_done, TC * (4 * b + NC + c + 1))
                sp.dma_start(out_v[b, :, TC * c:TC * (c + 1), :],
                             x1[:, TC * c:TC * (c + 1), :]).then_inc(out_stored, 16)

            def walk(plan, b, nxt, bank, further=True):
                for what, *n in plan:
                    if what == "load_xT" and further:
                        load_xT(nxt + 1)
                    elif what == "load_x" and nxt is not None:
                        load_x(nxt)
                    elif what == "stack":
                        stack(n[0], nxt, bank)
                    elif what == "store":
                        store(n[0], b)

            sp.dma_start(xT_sb[:, :, :], xT_v[0, :, :, :]).then_inc(xT_in, 16)
            sp.dma_start(wvp_sb[:, :, 0:D], Wv.rearrange("(k p) n -> p k n", p=P)).then_inc(weights_in, 16)
            sp.dma_start(wvp_sb[:, :, D:VZ], Wp.rearrange("(k p) n -> p k n", p=P)).then_inc(weights_in, 16)
            sp.dma_start(bp_sb[:, :], bp.rearrange("(a n) -> a n", a=1).partition_broadcast(P)).then_inc(weights_in, 16)
            for n, w in enumerate((wgT, wuT)):
                sp.dma_start(w_int[n].rearrange("p (k n) -> p k n", k=KD),
                             w.rearrange("(k p) n -> p k n", p=P)).then_inc(ints_in, 16)
            sp.dma_start(w_int[2].rearrange("p (m n) -> p m n", m=M1),
                         wdT.rearrange("(m p) n -> p m n", p=P)).then_inc(ints_in, 16)
            sp.dma_start(wo_sb[:, :, :], Wo.rearrange("(k p) n -> p k n", p=P)).then_inc(wo_in, 16)
            sp.dma_start(x_sb[:, :, :], x_v[0, :, :, :]).then_inc(x_in, 16)
            walk(START, None, 0, start_bank)
            with sp.Fori(0, B - 2) as b:
                walk(BODY, b, b + 1, body_bank(b))
            walk(BODY, B - 2, B - 1, body_bank(B - 2), further=False)
            walk(END, B - 1, None, end_bank)
            sp.wait_ge(out_stored, 16 * NC * B)

        @block.gpsimd
        def _(pool):
            pool.memset(ident[:, :], 0.0).then_inc(ident_ready, 1)
            pool.memset(neg_half[:, :], -0.5).then_inc(consts_ready, 1)
            pool.memset(ones[:, :], 1.0).then_inc(consts_ready, 1)
            pool.wait_ge(ident_ready, 1)
            pool.affine_select(out=ident[:, :], in_=ident[:, :], compare_op=ALU.not_equal, fill=1.0,
                               base=0, pattern=[[-1, P]], channel_multiplier=1).then_inc(ident_ready, 1)

            def mask(i, b):
                q, c, g, j = STEPS[i]
                off = P * j - CH * c
                exps_done = [pool.compute_val(SLOT_USES[p] * b + i + 1) for p in range(2)]
                pool.wait_ge(ident_ready, 2)
                pool.wait_ge(slot_drained[0], exps_done[0])
                pool.wait_ge(slot_drained[1], exps_done[1])
                tile = probs[:, i % P_SLOTS, :, off:off + P]
                pool.affine_select(out=tile, in_=tile, compare_op=ALU.is_ge, fill=0.0, base=0,
                                   pattern=[[0, 4], [1, P]], channel_multiplier=-1).then_inc(masked, 1)

            def rsqrt(n, b):
                pool.wait_ge(var_ready, 4 * b + n + 1)
                pool.tensor_tensor(rstd[:, :], var_eps[:, :], neg_half[:, :], ALU.pow).then_inc(rstd_ready, 1)

            def hidden_lo(n, b):
                pool.wait_ge(hid_hi_ready, GATES * b + n + 1)
                pool.tensor_tensor(hid_lo[:, n // M1, n % M1, :], hid[:, n % HSLOTS, :],
                                   hid_hi[:, n // M1, n % M1, :], ALU.subtract).then_inc(hid_lo_ready, 1)

            def walk(plan, b, nxt):
                for what, *n in plan:
                    if what == "mask":
                        mask(n[0], nxt)
                    elif what == "rsqrt":
                        rsqrt(n[0], nxt if n[0] == 0 else b)
                    elif what == "hidden_lo":
                        hidden_lo(n[0], b)
                    elif what == "weights":
                        pool.wait_ge(w_max_ready, 4)
                        pool.partition_all_reduce(w_gmax[:, :], w_max[:, :], P, RMAX).then_inc(w_gmax_ready, 1)

            walk(START, None, 0)
            with pool.Fori(0, B - 1) as b:
                walk(BODY, b, b + 1)
            walk(END, B - 1, None)

        @block.scalar
        def _(act):
            def vz_out(t, bank):
                k, n = bank(f"vz{t}")
                act.wait_ge(misc_filled[k], n + 1)
                act.activation(vz_sb[:, t, :], misc[k][:, 0:VZ], ACT.Copy).then_inc(misc_drained[k], 1)

            def squash(h, b):
                act.wait_ge(z_ready, 2 * b + h + 1)
                act.activation(u_sb[:, HT * H * h:HT * H * (h + 1), :].rearrange("p a d -> p (a d)"),
                               z_sb[:, HT * h:HT * (h + 1), :].rearrange("p t n -> p (t n)"),
                               ACT.Tanh, scale=0.5).then_inc(u_ready, 1)

            def phi_high(g, c, b, bank):
                k, n = bank(f"f{g}{c}")
                act.wait_ge(misc_filled[k], n + 1)
                if g == 0 and c == 0:
                    act.wait_ge(scale_ready, 1)
                    if bank is not start_bank:
                        for s in range(NG):
                            act.wait_ge(stacks_in[s], 16 * STACK_DMAS * b)
                act.activation(phi_hi[:, g, CH * c:CH * (c + 1)], misc[k][:, :], ACT.Copy,
                               scale=feat_scale[:, 0:1]).then_inc(phi_hi_ready, 1)

            def exps(i, b):
                q, c, g, j = STEPS[i]
                off = max(P * j - CH * c, 0)
                if i >= P_SLOTS:
                    act.wait_ge(pv_done, NS * b + i - P_SLOTS + 1)
                for p in range(2):
                    act.wait_ge(slot_filled[p], SLOT_USES[p] * b + i + 1)
                    act.activation(probs[:, i % P_SLOTS, 2 * p:2 * p + 2, off:CH],
                                   slot[p][:, :, off:CH], ACT.Exp).then_inc(slot_drained[p], 1)

            def x1_high(c, bank):
                for k2 in range(KD):
                    k, n = bank(f"x{c}{k2}")
                    act.wait_ge(misc_filled[k], n + 1)
                    act.activation(x1T_hi[:, k2, CH * c:CH * (c + 1)], misc[k][:, :],
                                   ACT.Copy).then_inc(x1T_hi_ready, 1)

            def gate_tanh(n, b):
                s, uses = gate_slot(n, b)
                act.wait_ge(slot_filled[s], uses + 1)
                act.activation(tanh_g[:, n % 2, :], slot[s][:, 0, :], ACT.Tanh,
                               scale=0.5 * QUANT).then_inc(tanh_ready, 1)

            def hidden_hi(n, b):
                s, uses = gate_slot(n, b)
                act.wait_ge(slot_drained[s], uses + 1)
                act.activation(hid_hi[:, n // M1, n % M1, :], hid[:, n % HSLOTS, :],
                               ACT.Copy).then_inc(hid_hi_ready, 1)

            def walk(plan, b, nxt, bank):
                for what, *n in plan:
                    if what == "vz_out":
                        vz_out(n[0], bank)
                    elif what == "squash":
                        squash(n[0], nxt)
                    elif what == "phi_high":
                        phi_high(*n, nxt, bank)
                    elif what == "exps":
                        exps(n[0], nxt)
                    elif what == "x1_high":
                        x1_high(n[0], bank)
                    elif what == "tanh":
                        gate_tanh(n[0], b)
                    elif what == "hidden_hi":
                        hidden_hi(n[0], b)

            walk(START, None, 0, start_bank)
            with act.Fori(0, B - 1) as b:
                walk(BODY, b, b + 1, body_bank(b))
            walk(END, B - 1, None, end_bank)

        @block.vector
        def _(dve):
            def bias_add(h, bank):
                for t in (HT * (h + 1) - 2, HT * (h + 1) - 1):
                    k, n = bank(f"vz{t}")
                    dve.wait_ge(misc_drained[k], n + 1)
                dve.tensor_tensor(z_sb[:, HT * h:HT * (h + 1), :], vz_sb[:, HT * h:HT * (h + 1), D:VZ],
                                  bp_sb[:, :].rearrange("p (a n) -> p a n", a=1).to_broadcast([P, HT, HD]),
                                  ALU.add).then_inc(z_ready, 1)

            def features(h, b):
                rows = slice(HT * H * h, HT * H * (h + 1))
                dve.wait_ge(u_ready, 2 * b + h + 1)
                for m in range(DEPTH):
                    w = 2 ** m
                    if m >= 1:
                        dve.wait_ge(feat_ready, DEPTH * (2 * b + h) + m)
                    dve.tensor_tensor(feat[:, rows, w:2 * w], feat[:, rows, 0:w],
                                      u_sb[:, rows, m:m + 1].to_broadcast([P, HT * H, w]),
                                      ALU.mult).then_inc(feat_ready, 1)

            def phi_low(g, c, b, bank):
                k, n = bank(f"f{g}{c}")
                cols = slice(CH * c, CH * (c + 1))
                dve.wait_ge(phi_hi_ready, NG * NC * b + NC * g + c + 1)
                dve.scalar_tensor_tensor(out=phi_lo[:, g, cols], in0=misc[k][:, :],
                                         scalar=feat_scale[:, 0:1], in1=phi_hi[:, g, cols],
                                         op0=ALU.mult, op1=ALU.subtract).then_inc(misc_drained[k], 1)

            def normalise(q, b):
                c, g = CHUNKS[q]
                dve.wait_ge(pv_done, NS * b + LAST[q] + 1)
                if q >= 1:
                    dve.wait_ge(ctxT_ready, NQ * b + q)
                dve.tensor_copy(ctx_raw[:, :], ctx_ps).then_inc(ctx_out, 1)
                dve.transpose(den_turned[:, :, :].rearrange("p a n -> p (a n)"), den_ps).then_inc(den_out, 1)
                dve.wait_ge(den_out, NQ * b + q + 1)
                dve.reciprocal(den_recip[:, :, :], den_turned[:, :, 0:1]).then_inc(den_recip_ready, 1)
                dve.wait_ge(den_recip_ready, NQ * b + q + 1)
                dve.transpose(den_inv[:, :].rearrange("p (a n) -> p a n", n=32),
                              den_recip[:, :, :].to_broadcast([P, CH // 32, 32])).then_inc(den_inv_ready, 1)
                dve.wait_ge(den_inv_ready, NQ * b + q + 1)
                dve.wait_ge(ctx_out, NQ * b + q + 1)
                dve.tensor_tensor(ctxT[:, g, :], ctx_raw[:, :], den_inv[:, :], ALU.mult)\
                    .then_inc(ctxT_ready, 1)

            def residual(c, b, bank):
                for s in range(TC // 2):
                    k, n = bank(f"o{c}{s}")
                    t = TC * c + 2 * s
                    dve.wait_ge(misc_filled[k], n + 1)
                    if s == 0 and c == 0:
                        dve.wait_ge(x_in, 16 * (b + 1))
                    dve.tensor_tensor(x1[:, t:t + 2, :], misc[k][:, :].rearrange("p (t n) -> p t n", t=2),
                                      x_sb[:, t:t + 2, :], ALU.add).then_inc(misc_drained[k], 1)

            def ffn_residual(c, bank):
                for s in range(TC // 2):
                    k, n = bank(f"d{c}{s}")
                    t = TC * c + 2 * s
                    dve.wait_ge(misc_filled[k], n + 1)
                    dve.scalar_tensor_tensor(out=x1[:, t:t + 2, :].rearrange("p t n -> p (t n)"),
                                             in0=misc[k][:, :], scalar=out_scale[:, 0:1],
                                             in1=x1[:, t:t + 2, :].rearrange("p t n -> p (t n)"),
                                             op0=ALU.mult, op1=ALU.add).then_inc(misc_drained[k], 1)

            def stats(ln, b, bank):
                c = ln % NC
                rows_before = TC * (4 * b + ln)
                if not (isinstance(rows_before, int) and rows_before == 0):
                    dve.wait_ge(ln_done, rows_before)
                for s in range(TC // 2):
                    k, n = bank(f"{'od'[ln // NC]}{c}{s}")
                    dve.wait_ge(misc_drained[k], n + 1)
                    for t in (2 * s, 2 * s + 1):
                        dve.bn_stats(bn[:, t, :], x1[:, TC * c + t, :]).then_inc(bn_ready, 1)
                rows_done = dve.compute_val(TC * (4 * b + ln + 1))
                dve.wait_ge(weights_in, 16 * 3)
                dve.wait_ge(bn_ready, rows_done)
                for t in range(TC):
                    dve.bn_aggr(mv[:, t, :], bn[:, t, :]).then_inc(mv_ready, 1)
                dve.wait_ge(mv_ready, TC * (4 * b + ln + 1))
                dve.tensor_scalar(var_eps[:, :], mv[:, :, 1], EPS, None, ALU.add).then_inc(var_ready, 1)

            def apply(ln, b):
                dve.wait_ge(rstd_ready, 4 * b + ln + 1)
                for t in range(TC):
                    row = x1[:, TC * (ln % NC) + t, :]
                    dve.tensor_scalar(row, row, mv[:, t, 0:1], rstd[:, t:t + 1],
                                      ALU.subtract, ALU.mult).then_inc(ln_done, 1)

            def x1_low(c, b, bank):
                for k2 in range(KD):
                    k, n = bank(f"x{c}{k2}")
                    cols = slice(CH * c, CH * (c + 1))
                    dve.wait_ge(x1T_hi_ready, NC * KD * b + KD * c + k2 + 1)
                    dve.tensor_tensor(x1T_lo[:, k2, cols], misc[k][:, :], x1T_hi[:, k2, cols],
                                      ALU.subtract).then_inc(misc_drained[k], 1)

            def hidden(n, b):
                s, uses = gate_slot(n, b)
                dve.wait_ge(tanh_ready, GATES * b + n + 1)
                if n >= 2:
                    s2, uses2 = gate_slot(n - 2, b)
                    dve.wait_ge(slot_drained[s2], uses2 + 1)
                dve.scalar_tensor_tensor(out=gated[:, n % 2, :], in0=tanh_g[:, n % 2, :], scalar=1.0,
                                         in1=slot[s][:, 0, :], op0=ALU.add, op1=ALU.mult)\
                    .then_inc(gated_ready, 1)
                dve.wait_ge(gated_ready, GATES * b + n + 1)
                if n >= HSLOTS:
                    dve.wait_ge(hid_lo_ready, GATES * b + n - HSLOTS + 1)
                dve.scalar_tensor_tensor(out=hid[:, n % HSLOTS, :], in0=gated[:, n % 2, :],
                                         scalar=hid_scale[:, 0:1], in1=slot[s][:, 1, :],
                                         op0=ALU.mult, op1=ALU.mult).then_inc(slot_drained[s], 1)

            def constants():
                dve.memset(feat[:, :, 0:1], 1.0)
                row = scale_row[:, :].rearrange("a (h f) -> a h f", h=4)
                for m in range(DEPTH + 1):
                    c_m = sum(2.0 ** -l for l in range(max(m, 1), DEPTH + 1)) / DEPTH
                    lo, hi = (0, 1) if m == 0 else (2 ** (m - 1), 2 ** m)
                    ins = dve.memset(row[:, :, lo:hi], c_m ** 0.5)
                ins.then_inc(consts_ready, 1)
                k, n = start_bank("scale")
                dve.wait_ge(misc_filled[k], n + 1)
                dve.tensor_copy(feat_scale[:, :], misc[k][:, 0:1]).then_inc(misc_drained[k], 1)
                dve.wait_ge(misc_drained[k], n + 1)
                dve.sem_inc(scale_ready, 1)
                dve.wait_ge(weights_in, 16 * 3)

            def split_weights():
                dve.wait_ge(ints_in, 16 * 3)
                for n in range(3):
                    dve.tensor_copy(w_parts[:, n, 0, :], w_int[n]).then_inc(split_step, 1)
                    dve.tensor_reduce(w_max[:, n:n + 1], w_int[n], AX.X, ALU.max,
                                      apply_absolute_value=True).then_inc(w_max_ready, 1)
                    dve.wait_ge(split_step, 3 * n + 1)
                    dve.tensor_tensor(w_rest[:, :], w_int[n], w_parts[:, n, 0, :], ALU.subtract)\
                        .then_inc(split_step, 1)
                    dve.wait_ge(split_step, 3 * n + 2)
                    dve.tensor_reduce(rest_max[:, n:n + 1], w_rest[:, :], AX.X, ALU.max,
                                      apply_absolute_value=True).then_inc(split_step, 1)
                    dve.wait_ge(split_step, 3 * n + 3)
                dve.tensor_reduce(w_max[:, 3:4], rest_max[:, :], AX.X, ALU.max).then_inc(w_max_ready, 1)

                dve.wait_ge(w_gmax_ready, 1)
                chain = 0

                def scaled(ins):
                    nonlocal chain
                    chain += 1
                    ins.then_inc(ffn_scale_step, 1)
                    dve.wait_ge(ffn_scale_step, chain)

                scaled(dve.tensor_scalar(w_one[:, :], w_gmax[:, 0:2], 1.0, None, ALU.max))
                scaled(dve.tensor_tensor(w_prod[:, :], w_one[:, 0:1], w_one[:, 1:2], ALU.mult))
                scaled(dve.reciprocal(w_inv[:, :], w_prod[:, :]))
                scaled(dve.tensor_scalar(hid_scale[:, :], w_inv[:, :], 0.25, None, ALU.mult))
                scaled(dve.tensor_scalar(out_scale[:, :], w_prod[:, :], 2.0 * QUANT ** 3, None, ALU.mult))
                scaled(dve.tensor_scalar(wide[:, :], w_gmax[0:1, 3:4], 0.0, None, ALU.is_gt))
                rest_left = dve.value_load(wide[0:1, 0:1], min_val=0, max_val=1)
                with dve.If(rest_left == 1):
                    steps = 9
                    for n in range(3):
                        dve.tensor_tensor(w_rest[:, :], w_int[n], w_parts[:, n, 0, :], ALU.subtract)\
                            .then_inc(split_step, 1)
                        dve.wait_ge(split_step, steps + 4 * n + 1)
                        dve.tensor_copy(w_parts[:, n, 1, :], w_rest[:, :]).then_inc(split_step, 1)
                        dve.wait_ge(split_step, steps + 4 * n + 2)
                        dve.tensor_tensor(w_rest[:, :], w_rest[:, :], w_parts[:, n, 1, :], ALU.subtract)\
                            .then_inc(split_step, 1)
                        dve.wait_ge(split_step, steps + 4 * n + 3)
                        dve.tensor_copy(w_parts[:, n, 2, :], w_rest[:, :]).then_inc(split_step, 1)
                        dve.wait_ge(split_step, steps + 4 * n + 4)
                dve.end_ifs()
                dve.tensor_copy(w_one[:, :], w_gmax[:, 0:2]).then_inc(weights_split, 1)

            def walk(plan, b, nxt, bank):
                for what, *n in plan:
                    if what == "scale":
                        constants()
                    elif what == "bias":
                        bias_add(n[0], bank)
                    elif what == "features":
                        features(n[0], nxt)
                    elif what == "phi_low":
                        phi_low(*n, nxt, bank)
                    elif what == "weights":
                        split_weights()
                    elif what == "normalise":
                        normalise(n[0], nxt)
                    elif what == "residual":
                        residual(n[0], nxt if n[0] == 0 else b, bank)
                    elif what == "stats":
                        stats(n[0], nxt if n[0] == 0 else b, bank)
                    elif what == "apply":
                        apply(n[0], nxt if n[0] == 0 else b)
                    elif what == "x1_low":
                        x1_low(n[0], nxt if n[0] == 0 else b, bank)
                    elif what == "hidden":
                        hidden(n[0], b)
                    elif what == "ffn_residual":
                        ffn_residual(n[0], bank)

            walk(START, None, 0, start_bank)
            with dve.Fori(0, B - 1) as b:
                walk(BODY, b, b + 1, body_bank(b))
            walk(END, B - 1, None, end_bank)

        @block.tensor
        def _(pe):
            def claim(name, bank):
                k, n = bank(name)
                if not (isinstance(n, int) and n == 0):
                    pe.wait_ge(misc_drained[k], n)
                return k

            def project_in(t, b, bank):
                k = claim(f"vz{t}", bank)
                if t == 0:
                    pe.wait_ge(xT_in, 16 * (b + 1))
                for d in range(KD):
                    mm = pe.matmul(misc[k][:, 0:VZ], xT_sb[:, d, t * P:(t + 1) * P], wvp_sb[:, d, :],
                                   start=(d == 0), stop=(d == KD - 1))
                mm.then_inc(misc_filled[k], 1)

            def turn_features(g, c, b, bank):
                pe.wait_ge(feat_ready, DEPTH * (2 * b + c + 1))
                tiles = feat[:, :, :].rearrange("p (t h) f -> p t (h f)", h=H)
                k = claim(f"f{g}{c}", bank)
                for t in range(TC):
                    mm = pe.transpose(misc[k][:, t * P:(t + 1) * P],
                                      tiles[:, TC * c + t, g * P:(g + 1) * P], ident[:, :])
                mm.then_inc(misc_filled[k], 1)

            def scores(i, b):
                q, c, g, j = STEPS[i]
                off = max(P * j - CH * c, 0)
                if c == 0 and j == 0:
                    pe.wait_ge(stacks_in[g], 16 * STACK_DMAS * (b + 1))
                for p in range(2):
                    uses = SLOT_USES[p] * b + i
                    if not (isinstance(uses, int) and uses == 0):
                        pe.wait_ge(slot_drained[p], uses)
                    for s in range(2):
                        h = 4 * g + 2 * p + s
                        mm = pe.matmul(slot[p][:, s, off:CH], key_stack[:, h, P * j:P * (j + 1)],
                                       query_stack[:, h, CH * c + off:CH * (c + 1)], start=True, stop=True)
                    mm.then_inc(slot_filled[p], 1)

            def weigh(i, b):
                q, c, g, j = STEPS[i]
                off = max(P * j - CH * c, 0)
                first, final = j == 0, j == TC * (c + 1) - 1
                if i == 0:
                    pe.wait_ge(u_ready, 2 * (b + 1))
                for p in range(2):
                    pe.wait_ge(slot_drained[p], SLOT_USES[p] * b + i + 1)
                if i in DIAG:
                    pe.wait_ge(masked, len(DIAG) * b + DIAG.index(i) + 1)
                for sums, taken in ((ctx_ps, ctx_out), (den_ps, den_out)):
                    if first and q >= 1:
                        pe.wait_ge(taken, NQ * b + q)
                    for s in range(4):
                        h = 4 * g + s
                        w = vz_sb[:, j, 32 * h:32 * h + 32] if taken is ctx_out else ones[:, :]
                        mm = pe.matmul(sums[32 * s:32 * s + 32, off:CH], w,
                                       probs[:, i % P_SLOTS, s, off:CH], start=first, stop=final)
                mm.then_inc(pv_done, 1)

            def project(c, b, bank):
                pe.wait_ge(ctxT_ready, NQ * b + NG * (c + 1))
                if c == 0:
                    pe.wait_ge(wo_in, 16)
                for s in range(TC // 2):
                    k = claim(f"o{c}{s}", bank)
                    for t in (2 * s, 2 * s + 1):
                        for g in range(NG):
                            mm = pe.matmul(misc[k][:, (t % 2) * D:(t % 2 + 1) * D],
                                           ctxT[:, g, t * P:(t + 1) * P], wo_sb[:, g, :],
                                           start=(g == 0), stop=(g == NG - 1))
                    mm.then_inc(misc_filled[k], 1)

            def turn_x1(c, b, bank):
                pe.wait_ge(ln_done, TC * (4 * b + c + 1))
                for k2 in range(KD):
                    k = claim(f"x{c}{k2}", bank)
                    for t in range(TC):
                        mm = pe.transpose(misc[k][:, t * P:(t + 1) * P],
                                          x1[:, TC * c + t, k2 * P:(k2 + 1) * P], ident[:, :])
                    mm.then_inc(misc_filled[k], 1)

            def gate_up(n, b, bank, parts):
                c, m = divmod(n, M1)
                if n == M1:
                    for k2 in range(KD):
                        k, u = bank(f"x{c}{k2}")
                        pe.wait_ge(misc_drained[k], u + 1)
                s, uses = gate_slot(n, b)
                if s < 2 or n >= SLOTS:
                    pe.wait_ge(slot_drained[s], uses)
                else:
                    pe.wait_ge(ctx_out, NQ * (b + 1))
                    pe.wait_ge(den_out, NQ * (b + 1))
                for w in range(2):
                    terms = [(a, k, d) for k in range(parts) for d in range(KD) for a in (x1T_hi, x1T_lo)]
                    for e, (a, k, d) in enumerate(terms):
                        mm = pe.matmul(slot[s][:, w, :], w_parts[:, w, k, d * F + m * P:d * F + (m + 1) * P],
                                       a[:, d, CH * c:CH * (c + 1)], start=(e == 0), stop=(e == len(terms) - 1))
                mm.then_inc(slot_filled[s], 1)

            def down(c, b, bank, parts):
                pe.wait_ge(hid_lo_ready, GATES * b + M1 * (c + 1))
                for s in range(TC // 2):
                    k = claim(f"d{c}{s}", bank)
                    for t in (2 * s, 2 * s + 1):
                        terms = [(a, w, m) for w in range(parts) for m in range(M1) for a in (hid_hi, hid_lo)]
                        for e, (a, w, m) in enumerate(terms):
                            mm = pe.matmul(misc[k][:, (t % 2) * D:(t % 2 + 1) * D],
                                           a[:, c, m, t * P:(t + 1) * P],
                                           w_parts[:, 2, w, m * D:(m + 1) * D],
                                           start=(e == 0), stop=(e == len(terms) - 1))
                    mm.then_inc(misc_filled[k], 1)

            def walk(plan, b, nxt, bank, parts=None):
                for what, *n in plan:
                    if what == "scale":
                        pe.wait_ge(consts_ready, 3)
                        pe.wait_ge(ident_ready, 2)
                        k, _ = bank("scale")
                        pe.matmul(misc[k][:, 0:1], scale_row[:, :], ones[0:1, 0:1], start=True, stop=True)\
                            .then_inc(misc_filled[k], 1)
                        pe.wait_ge(weights_in, 16 * 3)
                    elif what == "vz":
                        project_in(n[0], nxt, bank)
                    elif what == "turn_features":
                        turn_features(*n, nxt, bank)
                    elif what == "scores":
                        scores(n[0], nxt)
                    elif what == "weigh":
                        weigh(n[0], nxt)
                    elif what == "project":
                        project(n[0], nxt if n[0] == 0 else b, bank)
                    elif what == "turn_x1":
                        turn_x1(n[0], nxt if n[0] == 0 else b, bank)
                    elif what == "gate_up":
                        gate_up(n[0], b, bank, parts)
                    elif what == "down":
                        down(n[0], b, bank, parts)

            def feed_forward(plan, b, nxt, bank):
                rest_left = pe.value_load(wide[0:1, 0:1], min_val=0, max_val=1)
                with pe.If(rest_left == 0):
                    walk(plan, b, nxt, bank, 1)
                with pe.Else():
                    walk(plan, b, nxt, bank, 3)

            walk(START, None, 0, start_bank)
            pe.wait_ge(weights_split, 1)
            with pe.Fori(0, B - 1) as b:
                feed_forward(after_attention(True), b, b + 1, body_bank(b))
                walk(attention(False), b, b + 1, body_bank(b))
            feed_forward(END, B - 1, None, end_bank)


LAST_NORM_AT = 5
PROJECT_AT = 12
X1_AT = 18
X1_TURN_AT = 5
DOWN0_AT = 8

_OUTS = [((8, 1024, 256), 'float32')]


def kernel(L0_attn_x, L0_attn_Wp, L0_attn_bp, L0_attn_Wv, L0_attn_Wo, L0_ffn_w_gate, L0_ffn_w_up, L0_ffn_w_down):
    import numpy as _np
    import concourse.bacc as _bacc
    from concourse import mybir as _mybir
    from concourse.bass_utils import run_bass_kernel_spmd as _run

    lay = {
        "x": L0_attn_x,
        "xT": _np.asarray(L0_attn_x).transpose(0, 2, 1),
        "Wp": L0_attn_Wp, "bp": L0_attn_bp, "Wv": L0_attn_Wv, "Wo": L0_attn_Wo,
        "wgT": _np.asarray(L0_ffn_w_gate).T, "wuT": _np.asarray(L0_ffn_w_up).T,
        "wdT": _np.asarray(L0_ffn_w_down).T,
    }
    nc = _bacc.Bacc("TRN2", target_bir_lowering=False, num_devices=1)
    arrays, args = {}, []
    for name, a in lay.items():
        a = _np.ascontiguousarray(a)
        arrays[f"in_{name}_dram"] = a
        args.append(nc.dram_tensor(f"in_{name}_dram", a.shape, _mybir.dt.from_np(a.dtype), kind="ExternalInput").ap())
    for i, (shape, dtype) in enumerate(_OUTS):
        dt = _mybir.dt.from_np(_np.dtype(dtype))
        args.append(nc.dram_tensor(f"out_{i}_dram", shape, dt, kind="ExternalOutput").ap())
    seq_postln_kernel(nc, *args)
    r = _run(nc, [arrays], core_ids=[0])
    return r.results[0]["out_0_dram"]
```
